# Optimizing a Trainium2 kernel written in Bass

```python
import numpy as np
import jax
import jax.numpy as jnp

def _softmax(x, axis=-1):
    return jax.nn.softmax(x, axis=axis)

def _gelu(x):
    return jax.nn.gelu(x, approximate=True)

def _silu(x):
    return jax.nn.silu(x)

def _sigmoid(x):
    return jax.nn.sigmoid(x)

def _layernorm(x, axis=-1, eps=1e-05):
    m = jnp.mean(x, axis=axis, keepdims=True)
    v = jnp.var(x, axis=axis, keepdims=True)
    return (x - m) / jnp.sqrt(v + eps)

def _scatter_add(tgt, idx, src, axis=0):
    return tgt.at[idx].add(src)

def _segment_sum(src, seg, n):
    return jax.ops.segment_sum(src, seg, n)
kernel_name = 'mk_dlrm_tower_d1_rec_r8_1a3c7e'

def setup_inputs(seed: int=0):
    np.random.seed(seed)
    _w = jnp.asarray

    def _rec_inputs():
        import jax
        import jax.numpy as jnp
        _tk = jax.random.key(seed)
        dense_ctx = jax.random.normal(jax.random.fold_in(_tk, 190), (1024, 16), jnp.float32)
        ids = jnp.stack([jax.random.randint(jax.random.fold_in(_tk, 200 + f), (1024,), 0, v, jnp.int32) for f, v in enumerate([12500, 1000, 1250, 12500, 1250, 1250, 125000, 1250, 1250, 1250, 1250, 1250, 1250, 125000, 12500, 1250, 125000, 1250, 1250, 1000, 12500, 12500, 12500, 1000, 1250, 1250, 12500, 1000, 1000, 1000, 1250, 1250])], axis=1)
        tbl_0 = 0.05 * jax.random.normal(jax.random.fold_in(_tk, 500 + 0), (12500, 64), jnp.float32)
        tbl_1 = 0.05 * jax.random.normal(jax.random.fold_in(_tk, 500 + 1), (1000, 64), jnp.float32)
        tbl_2 = 0.05 * jax.random.normal(jax.random.fold_in(_tk, 500 + 2), (1250, 64), jnp.float32)
        tbl_3 = 0.05 * jax.random.normal(jax.random.fold_in(_tk, 500 + 3), (12500, 64), jnp.float32)
        tbl_4 = 0.05 * jax.random.normal(jax.random.fold_in(_tk, 500 + 4), (1250, 64), jnp.float32)
        tbl_5 = 0.05 * jax.random.normal(jax.random.fold_in(_tk, 500 + 5), (1250, 64), jnp.float32)
        tbl_6 = 0.05 * jax.random.normal(jax.random.fold_in(_tk, 500 + 6), (125000, 64), jnp.float32)
        tbl_7 = 0.05 * jax.random.normal(jax.random.fold_in(_tk, 500 + 7), (1250, 64), jnp.float32)
        tbl_8 = 0.05 * jax.random.normal(jax.random.fold_in(_tk, 500 + 8), (1250, 64), jnp.float32)
        tbl_9 = 0.05 * jax.random.normal(jax.random.fold_in(_tk, 500 + 9), (1250, 64), jnp.float32)
        tbl_10 = 0.05 * jax.random.normal(jax.random.fold_in(_tk, 500 + 10), (1250, 64), jnp.float32)
        tbl_11 = 0.05 * jax.random.normal(jax.random.fold_in(_tk, 500 + 11), (1250, 64), jnp.float32)
        tbl_12 = 0.05 * jax.random.normal(jax.random.fold_in(_tk, 500 + 12), (1250, 64), jnp.float32)
        tbl_13 = 0.05 * jax.random.normal(jax.random.fold_in(_tk, 500 + 13), (125000, 64), jnp.float32)
        tbl_14 = 0.05 * jax.random.normal(jax.random.fold_in(_tk, 500 + 14), (12500, 64), jnp.float32)
        tbl_15 = 0.05 * jax.random.normal(jax.random.fold_in(_tk, 500 + 15), (1250, 64), jnp.float32)
        tbl_16 = 0.05 * jax.random.normal(jax.random.fold_in(_tk, 500 + 16), (125000, 64), jnp.float32)
        tbl_17 = 0.05 * jax.random.normal(jax.random.fold_in(_tk, 500 + 17), (1250, 64), jnp.float32)
        tbl_18 = 0.05 * jax.random.normal(jax.random.fold_in(_tk, 500 + 18), (1250, 64), jnp.float32)
        tbl_19 = 0.05 * jax.random.normal(jax.random.fold_in(_tk, 500 + 19), (1000, 64), jnp.float32)
        tbl_20 = 0.05 * jax.random.normal(jax.random.fold_in(_tk, 500 + 20), (12500, 64), jnp.float32)
        tbl_21 = 0.05 * jax.random.normal(jax.random.fold_in(_tk, 500 + 21), (12500, 64), jnp.float32)
        tbl_22 = 0.05 * jax.random.normal(jax.random.fold_in(_tk, 500 + 22), (12500, 64), jnp.float32)
        tbl_23 = 0.05 * jax.random.normal(jax.random.fold_in(_tk, 500 + 23), (1000, 64), jnp.float32)
        tbl_24 = 0.05 * jax.random.normal(jax.random.fold_in(_tk, 500 + 24), (1250, 64), jnp.float32)
        tbl_25 = 0.05 * jax.random.normal(jax.random.fold_in(_tk, 500 + 25), (1250, 64), jnp.float32)
        tbl_26 = 0.05 * jax.random.normal(jax.random.fold_in(_tk, 500 + 26), (12500, 64), jnp.float32)
        tbl_27 = 0.05 * jax.random.normal(jax.random.fold_in(_tk, 500 + 27), (1000, 64), jnp.float32)
        tbl_28 = 0.05 * jax.random.normal(jax.random.fold_in(_tk, 500 + 28), (1000, 64), jnp.float32)
        tbl_29 = 0.05 * jax.random.normal(jax.random.fold_in(_tk, 500 + 29), (1000, 64), jnp.float32)
        tbl_30 = 0.05 * jax.random.normal(jax.random.fold_in(_tk, 500 + 30), (1250, 64), jnp.float32)
        tbl_31 = 0.05 * jax.random.normal(jax.random.fold_in(_tk, 500 + 31), (1250, 64), jnp.float32)
        _rk = jax.random.fold_in(_tk, 7)
        W_top1 = 0.0441942 * jax.random.normal(jax.random.fold_in(_tk, 801), (512, 512), jnp.float32)
        W_top2 = 0.0441942 * jax.random.normal(jax.random.fold_in(_tk, 802), (512, 256), jnp.float32)
        W_top3 = 0.0625 * jax.random.normal(jax.random.fold_in(_tk, 803), (256, 1), jnp.float32)
        b_top1 = jnp.zeros((512,), jnp.float32)
        b_top2 = jnp.zeros((256,), jnp.float32)
        return (dense_ctx, ids, tbl_0, tbl_1, tbl_2, tbl_3, tbl_4, tbl_5, tbl_6, tbl_7, tbl_8, tbl_9, tbl_10, tbl_11, tbl_12, tbl_13, tbl_14, tbl_15, tbl_16, tbl_17, tbl_18, tbl_19, tbl_20, tbl_21, tbl_22, tbl_23, tbl_24, tbl_25, tbl_26, tbl_27, tbl_28, tbl_29, tbl_30, tbl_31, W_top1, b_top1, W_top2, b_top2, W_top3)
    dense_ctx, ids, tbl_0, tbl_1, tbl_2, tbl_3, tbl_4, tbl_5, tbl_6, tbl_7, tbl_8, tbl_9, tbl_10, tbl_11, tbl_12, tbl_13, tbl_14, tbl_15, tbl_16, tbl_17, tbl_18, tbl_19, tbl_20, tbl_21, tbl_22, tbl_23, tbl_24, tbl_25, tbl_26, tbl_27, tbl_28, tbl_29, tbl_30, tbl_31, W_top1, b_top1, W_top2, b_top2, W_top3 = _rec_inputs()

    def _L0_rec_setup():
        import jax, jax.numpy as jnp
        import numpy as np
        FIELDS = 32
        EMBED = 64
        PAIRS = FIELDS * (FIELDS - 1) // 2
        BATCH = 256
        key = jax.random.key(seed)
        k1, k2 = jax.random.split(key)
        x = jax.random.normal(k1, (BATCH, FIELDS, EMBED), dtype=jnp.float32)
        kernel = jax.random.normal(k2, (EMBED, PAIRS, EMBED), dtype=jnp.float32) * 0.05
        return {'x': x, 'kernel': kernel}
    _L0_rec_all = _L0_rec_setup()
    _L0_rec_in = {k: v for k, v in _L0_rec_all.items() if k in ('kernel',)}
    del _L0_rec_all
    return {'dense_ctx': dense_ctx, 'ids': ids, 'tbl_0': tbl_0, 'tbl_1': tbl_1, 'tbl_2': tbl_2, 'tbl_3': tbl_3, 'tbl_4': tbl_4, 'tbl_5': tbl_5, 'tbl_6': tbl_6, 'tbl_7': tbl_7, 'tbl_8': tbl_8, 'tbl_9': tbl_9, 'tbl_10': tbl_10, 'tbl_11': tbl_11, 'tbl_12': tbl_12, 'tbl_13': tbl_13, 'tbl_14': tbl_14, 'tbl_15': tbl_15, 'tbl_16': tbl_16, 'tbl_17': tbl_17, 'tbl_18': tbl_18, 'tbl_19': tbl_19, 'tbl_20': tbl_20, 'tbl_21': tbl_21, 'tbl_22': tbl_22, 'tbl_23': tbl_23, 'tbl_24': tbl_24, 'tbl_25': tbl_25, 'tbl_26': tbl_26, 'tbl_27': tbl_27, 'tbl_28': tbl_28, 'tbl_29': tbl_29, 'tbl_30': tbl_30, 'tbl_31': tbl_31, 'W_top1': W_top1, 'b_top1': b_top1, 'W_top2': W_top2, 'b_top2': b_top2, 'W_top3': W_top3, 'L0_rec_kernel': _L0_rec_in['kernel']}

def reference(dense_ctx, ids, tbl_0, tbl_1, tbl_2, tbl_3, tbl_4, tbl_5, tbl_6, tbl_7, tbl_8, tbl_9, tbl_10, tbl_11, tbl_12, tbl_13, tbl_14, tbl_15, tbl_16, tbl_17, tbl_18, tbl_19, tbl_20, tbl_21, tbl_22, tbl_23, tbl_24, tbl_25, tbl_26, tbl_27, tbl_28, tbl_29, tbl_30, tbl_31, W_top1, b_top1, W_top2, b_top2, W_top3, L0_rec_kernel):
    import jax
    import jax.numpy as jnp

    def _L0_rec_ref(x, kernel):
        import jax, jax.numpy as jnp
        import numpy as np
        FIELDS = 32
        EMBED = 64
        PAIRS = FIELDS * (FIELDS - 1) // 2
        BATCH = 256
        iu, ju = jnp.triu_indices(FIELDS, k=1)
        p = x[:, iu, :]
        q = x[:, ju, :]
        result = jnp.einsum('bpe,fpe,bpf->bp', p, kernel, q)
        return result
    e = jnp.stack([tbl_0[ids[:, 0]], tbl_1[ids[:, 1]], tbl_2[ids[:, 2]], tbl_3[ids[:, 3]], tbl_4[ids[:, 4]], tbl_5[ids[:, 5]], tbl_6[ids[:, 6]], tbl_7[ids[:, 7]], tbl_8[ids[:, 8]], tbl_9[ids[:, 9]], tbl_10[ids[:, 10]], tbl_11[ids[:, 11]], tbl_12[ids[:, 12]], tbl_13[ids[:, 13]], tbl_14[ids[:, 14]], tbl_15[ids[:, 15]], tbl_16[ids[:, 16]], tbl_17[ids[:, 17]], tbl_18[ids[:, 18]], tbl_19[ids[:, 19]], tbl_20[ids[:, 20]], tbl_21[ids[:, 21]], tbl_22[ids[:, 22]], tbl_23[ids[:, 23]], tbl_24[ids[:, 24]], tbl_25[ids[:, 25]], tbl_26[ids[:, 26]], tbl_27[ids[:, 27]], tbl_28[ids[:, 28]], tbl_29[ids[:, 29]], tbl_30[ids[:, 30]], tbl_31[ids[:, 31]]], axis=1)
    z = _L0_rec_ref(e, L0_rec_kernel)
    z = z.reshape(z.shape[0], -1)
    h = jnp.concatenate([z, dense_ctx], axis=1)
    h = jnp.maximum(h @ W_top1 + b_top1, 0.0)
    h = jnp.maximum(h @ W_top2 + b_top2, 0.0)
    y = h @ W_top3
    return y

_drawn_inputs = setup_inputs


def setup_inputs(seed=0):
    import zlib

    import numpy as np

    out = dict(_drawn_inputs(seed))
    spreads = {'b_top1': (0.0, 0.1), 'b_top2': (0.0, 0.1)}
    factors = {'tbl_0': 6.197,
     'tbl_1': 6.113,
     'tbl_2': 5.718,
     'tbl_3': 5.913,
     'tbl_4': 4.778,
     'tbl_5': 6.412,
     'tbl_6': 5.676,
     'tbl_7': 4.985,
     'tbl_8': 5.711,
     'tbl_9': 5.567,
     'tbl_10': 5.607,
     'tbl_11': 5.314,
     'tbl_12': 5.136,
     'tbl_13': 5.064,
     'tbl_14': 5.751,
     'tbl_15': 5.475,
     'tbl_16': 5.1,
     'tbl_17': 5.818,
     'tbl_18': 5.001,
     'tbl_19': 5.562,
     'tbl_20': 5.455,
     'tbl_21': 5.715,
     'tbl_22': 6.205,
     'tbl_23': 5.841,
     'tbl_24': 5.831,
     'tbl_25': 5.346,
     'tbl_26': 5.593,
     'tbl_27': 5.615,
     'tbl_28': 5.826,
     'tbl_29': 5.536,
     'tbl_30': 5.4,
     'tbl_31': 6.05}
    for name, (base, spread) in spreads.items():
        noise = np.random.default_rng([zlib.crc32(name.encode()), seed]).standard_normal(out[name].shape)
        drawn = base * np.exp(spread * noise) if base else spread * noise
        out[name] = jnp.asarray(drawn.astype(out[name].dtype))
    for name, factor in factors.items():
        out[name] = (out[name] * factor).astype(out[name].dtype)
    return out
```

```python
import concourse.bass as bass
from concourse import mybir
from contextlib import ExitStack

BATCH, FIELDS, EMBED, DENSE = 1024, 32, 64, 16
H1, H2 = 512, 256
P = 128
HALVES = 2
HB = BATCH // HALVES
BT = HB // P
PACKS = FIELDS // 2
GC = 4
CHUNKS = PACKS * PACKS
GROUPS = CHUNKS // GC
TILE_CHUNKS = P // 2
ZT = CHUNKS // TILE_CHUNKS
KRING = 4
RAW = 8
PRING = 4


CREDIT = 1


def chunk_of(k, i):
    return k * k + i


def z_slot(c):
    return c // TILE_CHUNKS, c % 4, (c // 4) % 16


UNITS = [(k, tuple(i for i in (m, m + 1) if i <= 2 * k)) for k in range(PACKS) for m in range(0, 2 * k + 1, 2)]
NU = len(UNITS)
FIRST_UNIT = [min(u for u, (k, _) in enumerate(UNITS) if k == kk) for kk in range(PACKS)]
UNIT_OF_CHUNK = {chunk_of(k, i): u for u, (k, ii) in enumerate(UNITS) for i in ii}


def groups_due(u):
    def reach(v):
        return min(GROUPS, chunk_of(UNITS[v][0], UNITS[v][1][0]) // GC + 3)
    return range(reach(u - 1) if u else 0, reach(u))


def packs_due(u, lead):
    out = [0] if u == 0 else []
    k = UNITS[u][0]
    if k + 1 < PACKS and u == max(FIRST_UNIT[k], FIRST_UNIT[k + 1] - lead):
        out.append(k + 1)
    return out


def seen(h, per_half, v):
    return h * per_half + v if v >= 0 else h * (per_half + v)


def build(nc, ids, tables, kchunks, dense, w1, b1, w2, b2, w3, sel, sel_last, ident, y):
    fp32, f32r, i32 = mybir.dt.float32, mybir.dt.float32r, mybir.dt.int32
    ALU, ACT = mybir.AluOpType, mybir.ActivationFunctionType
    ctx = ExitStack()
    with ctx:
        def sb(name, shape, dt=fp32):
            return ctx.enter_context(nc.sbuf_tensor(name, shape, dt))

        def sem(name):
            return ctx.enter_context(nc.semaphore(name))

        ids_sb = sb("ids_sb", [P, BATCH // P, FIELDS], i32)
        ident_sb = sb("ident_sb", [P, P])
        sel_sb = sb("sel_sb", [P, 62])
        sel_last_sb = sb("sel_last_sb", [P, PACKS, 32])
        w1_sb = sb("w1_sb", [P, ZT, H1])
        w2_sb = sb("w2_sb", [P, H1 // P, H2])
        w3_sb = sb("w3_sb", [P, H2 // P])
        b1_sb = sb("b1_sb", [P, H1 // P])
        b2_sb = sb("b2_sb", [P, H2 // P])
        raw = sb("raw", [P, RAW, BT, 2, EMBED])
        parts = sb("parts", [P, BT, 2, 2, EMBED], f32r)
        xhl = sb("xhl", [P, FIELDS, HB], f32r)
        q = sb("q", [P, PACKS, HB])
        kraw = sb("kraw", [P, KRING, GC * P])
        khi = sb("khi", [P, KRING, GC * P], f32r)
        klo = sb("klo", [P, KRING, GC * P], f32r)
        prod = sb("prod", [P, PRING, 2, HB])
        prod_last = sb("prod_last", [P, 2, HB])
        zt = sb("zt", [P, ZT, HB])
        h1 = sb("h1", [P, H1 // P, HB])
        h2 = sb("h2", [P, H2 // P, HB])
        y_sb = sb("y_sb", [1, BATCH])

        t_ps = ctx.enter_context(nc.psum_tensor("t_ps", [P, 2, 2, HB], fp32))
        prep_ps = ctx.enter_context(nc.psum_tensor("prep_ps", [P, 2, HB], fp32))
        z_ps = ctx.enter_context(nc.psum_tensor("z_ps", [P, 2, HB], fp32))

        ids_in, consts_in, weights_in = sem("ids_in"), sem("consts_in"), sem("weights_in")
        dense_in = sem("dense_in")
        kraw_in = [sem(f"kraw_in{s}") for s in range(KRING)]
        gathered = [sem(f"gathered{s}") for s in range(RAW)]
        xhi_done, xlo_done = sem("xhi_done"), sem("xlo_done")
        transposed, prep_copied = sem("transposed"), sem("prep_copied")
        khi_done, klo_even, klo_odd = sem("khi_done"), sem("klo_even"), sem("klo_odd")
        t_done, prod_done, summed, z_copied = sem("t_done"), sem("prod_done"), sem("summed"), sem("z_copied")
        h1_done, h1_copied, h2_done, h2_copied = sem("h1_done"), sem("h1_copied"), sem("h2_done"), sem("h2_copied")
        y_done, y_copied, y_stored = sem("y_done"), sem("y_copied"), sem("y_stored")

        block = ctx.enter_context(nc.Block())

        @block.sync
        def _(sp):
            sp.dma_start(ids_sb[:], ids).then_inc(ids_in, 16)

            def load_group(h, g, slot, first=False):
                done = klo_odd if slot % 2 else klo_even
                if first:
                    sp.wait_ge(done, CREDIT + seen(h, GROUPS // 2, slot // 2 - 1))
                else:
                    sp.wait_ge(done, CREDIT + h * (GROUPS // 2) + g * 2 + (slot // 2 - 1))
                for lane in (0, EMBED):
                    sp.dma_start(kraw[lane:lane + EMBED, slot, :],
                                 kchunks[bass.ds(g * KRING + slot, 1), :, :].rearrange("g e n -> e (g n)")
                                 ).then_inc(kraw_in[slot], 16)

            with sp.Fori(0, HALVES) as h:
                for slot in range(KRING):
                    load_group(h, 0, slot, first=True)
                sp.wait_ge(summed, CREDIT + h * NU)
                for slot in range(2):
                    sp.dma_start(prod_last[0:EMBED, slot, :], dense[:, bass.ds(h * HB, HB)]).then_inc(dense_in, 16)
                with sp.Fori(1, GROUPS // KRING) as g:
                    for slot in range(KRING):
                        load_group(h, g, slot)

        @block.gpsimd
        def _(pool):
            def gather(pack):
                h, k = divmod(pack, PACKS)
                if pack >= RAW:
                    old = pack - RAW
                    pool.wait_ge(transposed, CREDIT + 3 * old + 1)
                    pool.wait_ge(xlo_done, old + 1)
                for f in range(2):
                    for t in range(BT):
                        nc.gpsimd.indirect_dma_start(
                            raw[:, pack % RAW, t, f, :], None, tables[2 * k + f],
                            bass.IndirectOffsetOnAxis(ap=ids_sb[:, h * BT + t, 2 * k + f:2 * k + f + 1], axis=0),
                        ).then_inc(gathered[pack % RAW], 16)

            pool.sem_inc(klo_odd, CREDIT)
            pool.wait_ge(ids_in, 16)
            issued = 0
            for h in range(HALVES):
                for u in range(NU):
                    k = UNITS[u][0]
                    target = PACKS * h + (min(k + RAW, k + 3 + 2 * max(0, k - 6)) if h == 0 else k + RAW)
                    target = min(target, HALVES * PACKS)
                    if u == 0 and h == 0:
                        target = 2
                    for g in groups_due(u):
                        if g % 2:
                            n = h * GROUPS + g
                            pool.wait_ge(khi_done, n + 1)
                            nc.gpsimd.tensor_tensor(klo[:, g % KRING, :], kraw[:, g % KRING, :],
                                                    khi[:, g % KRING, :].bitcast(fp32),
                                                    ALU.subtract).then_inc(klo_odd, 1)
                    while issued < target:
                        gather(issued)
                        issued += 1

        @block.scalar
        def _(act):
            act.sem_inc(y_copied, CREDIT)
            act.dma_start(ident_sb[:], ident).then_inc(consts_in, 16)
            act.dma_start(sel_sb[:], sel).then_inc(consts_in, 16)
            act.dma_start(sel_last_sb[:], sel_last).then_inc(consts_in, 16)
            for dst, src in ((w1_sb, w1), (w2_sb, w2), (w3_sb, w3), (b1_sb, b1), (b2_sb, b2)):
                act.dma_start(dst[:], src).then_inc(weights_in, 16)

            def split_group(h, g):
                act.wait_ge(kraw_in[g % KRING], h * (32 * GROUPS // KRING) + 32 * (g // KRING + 1))
                if g >= KRING:
                    act.wait_ge(t_done, h * NU + UNIT_OF_CHUNK[(g - KRING) * GC + GC - 1] + 1)
                nc.scalar.activation(khi[:, g % KRING, :], kraw[:, g % KRING, :], ACT.Copy).then_inc(khi_done, 1)

            def split_pack(h, k):
                act.wait_ge(gathered[k % RAW], h * (128 * PACKS // RAW) + 128 * (k // RAW + 1))
                act.wait_ge(transposed, CREDIT + h * (3 * PACKS) + 3 * k)
                nc.scalar.activation(parts[:, :, :, 0, :], raw[:, k % RAW], ACT.Copy).then_inc(xhi_done, 1)

            def copy_pack(h, k):
                for j in range(3):
                    act.wait_ge(transposed, CREDIT + h * (3 * PACKS) + 3 * k + j + 1)
                    dst = q[:, k, :] if j == 0 else xhl[:, 2 * k + j - 1, :]
                    nc.scalar.activation(dst, prep_ps[:, (3 * k + j) % 2, :], ACT.Copy).then_inc(prep_copied, 1)

            def copy_z(h, t):
                act.wait_ge(summed, CREDIT + h * NU + UNIT_OF_CHUNK[(t + 1) * TILE_CHUNKS - 1] + 1)
                nc.scalar.activation(zt[:, t, :], z_ps[:, t % 2, :], ACT.Copy).then_inc(z_copied, 1)

            z_at = {min(NU - 1, UNIT_OF_CHUNK[(t + 1) * TILE_CHUNKS - 1] + 4): t for t in range(ZT - 1)}
            with act.Fori(0, HALVES) as h:
                for u in range(NU):
                    for g in groups_due(u):
                        split_group(h, g)
                    splits, copies = packs_due(u, 5), packs_due(u, 3)
                    for k in sorted({*splits, *copies}):
                        if k in splits:
                            split_pack(h, k)
                        if k in copies:
                            copy_pack(h, k)
                    if u in z_at:
                        copy_z(h, z_at[u])
                copy_z(h, ZT - 1)
                act.wait_ge(weights_in, 80)
                for m in range(H1 // P):
                    act.wait_ge(h1_done, h * (H1 // P) + m + 1)
                    nc.scalar.activation(h1[:, m, :], t_ps[:, m // 2, m % 2, :], ACT.Relu,
                                         bias=b1_sb[:, m:m + 1]).then_inc(h1_copied, 1)
                for m in range(H2 // P):
                    act.wait_ge(h2_done, h * (H2 // P) + m + 1)
                    nc.scalar.activation(h2[:, m, :], t_ps[:, 0, m, :], ACT.Relu,
                                         bias=b2_sb[:, m:m + 1]).then_inc(h2_copied, 1)
                act.wait_ge(y_done, h + 1)
                nc.scalar.activation(y_sb[:, bass.ds(h * HB, HB)], t_ps[0:1, 1, 0, :], ACT.Copy).then_inc(y_copied, 1)
                act.wait_ge(y_copied, CREDIT + h + 1)
                act.dma_start(y[:, bass.ds(h * HB, HB)], y_sb[:, bass.ds(h * HB, HB)]).then_inc(y_stored, 16)
            act.wait_ge(y_stored, 16 * HALVES)

        @block.vector
        def _(dve):
            def split_pack(h, k):
                dve.wait_ge(xhi_done, h * PACKS + k + 1)
                nc.vector.tensor_tensor(parts[:, :, :, 1, :], raw[:, k % RAW], parts[:, :, :, 0, :].bitcast(fp32),
                                        ALU.subtract).then_inc(xlo_done, 1)

            def split_group(h, g):
                dve.wait_ge(khi_done, h * GROUPS + g + 1)
                nc.vector.tensor_tensor(klo[:, g % KRING, :], kraw[:, g % KRING, :],
                                        khi[:, g % KRING, :].bitcast(fp32), ALU.subtract).then_inc(klo_even, 1)

            def multiply(h, u):
                k, chunk_is = UNITS[u]
                dve.wait_ge(t_done, h * NU + u + 1)
                if len(chunk_is) == 2:
                    dve.wait_ge(summed, CREDIT + seen(h, NU, u - PRING + 1))
                    nc.vector.tensor_tensor(prod[:, u % PRING], t_ps[:, u % 2],
                                            q[:, k:k + 1, :].broadcast_to([P, 2, HB]), ALU.mult).then_inc(prod_done, 1)
                else:
                    if k >= 2:
                        dve.wait_ge(summed, CREDIT + h * NU + FIRST_UNIT[k - 1])
                    nc.vector.tensor_tensor(prod_last[EMBED:P, k % 2, :], t_ps[EMBED:P, u % 2, 0, :],
                                            q[EMBED:P, k, :], ALU.mult).then_inc(prod_done, 1)

            dve.sem_inc(klo_even, CREDIT)
            dve.sem_inc(prod_done, CREDIT)
            with dve.Fori(0, HALVES) as h:
                for u in range(NU):
                    for g in groups_due(u):
                        if g % 2 == 0:
                            split_group(h, g)
                    for k in packs_due(u, 5):
                        split_pack(h, k)
                    multiply(h, u)

        @block.tensor
        def _(pe):
            def prepare(h, k):
                for j in range(3):
                    if 3 * k + j >= 2:
                        pe.wait_ge(prep_copied, h * (3 * PACKS) + 3 * k + j - 1)
                    if j == 0:
                        pe.wait_ge(gathered[k % RAW], h * (128 * PACKS // RAW) + 128 * (k // RAW + 1))
                    if j == 1:
                        pe.wait_ge(xlo_done, h * PACKS + k + 1)
                    for t in range(BT):
                        src = raw[:, k % RAW, t, :, :] if j == 0 else parts[:, t, j - 1, :, :].bitcast(fp32)
                        last = nc.tensor.transpose(prep_ps[:, (3 * k + j) % 2, t * P:(t + 1) * P],
                                                   src.rearrange("p a e -> p (a e)"), ident_sb[:])
                    last.then_inc(transposed, 1)

            def bilinear(h, u):
                k, chunk_is = UNITS[u]
                if u == FIRST_UNIT[k]:
                    pe.wait_ge(prep_copied, h * (3 * PACKS) + 3 * k + 3)
                pe.wait_ge(prod_done, CREDIT + seen(h, NU, u - 1))
                for n, i in enumerate(chunk_is):
                    c = chunk_of(k, i)
                    g, at = divmod(c, GC)
                    if at == 0:
                        pe.wait_ge(klo_odd if g % 2 else klo_even, CREDIT + h * (GROUPS // 2) + g // 2 + 1)
                    for part, w in enumerate((khi, klo)):
                        last = nc.tensor.matmul(t_ps[:, u % 2, n, :], w[:, g % KRING, at * P:(at + 1) * P],
                                                xhl[:, i, :], start=(part == 0), stop=(part == 1))
                last.then_inc(t_done, 1)

            def feature_sums(h, u):
                k, chunk_is = UNITS[u]
                pe.wait_ge(prod_done, CREDIT + h * NU + u + 1)
                for n, i in enumerate(chunk_is):
                    tile, group, pos = z_slot(chunk_of(k, i))
                    if chunk_of(k, i) % TILE_CHUNKS == 0 and tile >= 2:
                        pe.wait_ge(z_copied, h * ZT + tile - 1)
                    last_chunk = i == 2 * k
                    w = sel_last_sb[:, k, :] if last_chunk else sel_sb[:, 30 - 2 * pos:62 - 2 * pos]
                    src = prod_last[:, k % 2, :] if last_chunk else prod[:, u % PRING, n, :]
                    last = nc.tensor.matmul(z_ps[32 * group:32 * group + 32, tile % 2, :], w, src,
                                            start=(pos == 0), stop=(pos == 15))
                last.then_inc(summed, 1)

            pe.sem_inc(summed, CREDIT)
            pe.sem_inc(transposed, CREDIT)
            pe.wait_ge(consts_in, 48)
            with pe.Fori(0, HALVES) as h:
                for u in range(NU):
                    for k in packs_due(u, 3):
                        prepare(h, k)
                    if u == 0:
                        pe.wait_ge(dense_in, h * 32 + 32)
                    if u == 1:
                        pe.wait_ge(y_copied, CREDIT + h)
                    bilinear(h, u)
                    if u % 2 and u >= 3:
                        feature_sums(h, u - 3)
                        feature_sums(h, u - 2)
                feature_sums(h, NU - 2)
                feature_sums(h, NU - 1)

                pe.wait_ge(weights_in, 80)
                pe.wait_ge(z_copied, h * ZT + ZT)
                for m in range(H1 // P):
                    for t in range(ZT):
                        last = nc.tensor.matmul(t_ps[:, m // 2, m % 2, :], w1_sb[:, t, m * P:(m + 1) * P],
                                                zt[:, t, :], start=(t == 0), stop=(t == ZT - 1))
                    last.then_inc(h1_done, 1)
                for m in range(H2 // P):
                    for t in range(H1 // P):
                        if m == 0:
                            pe.wait_ge(h1_copied, h * (H1 // P) + t + 1)
                        last = nc.tensor.matmul(t_ps[:, 0, m, :], w2_sb[:, t, m * P:(m + 1) * P],
                                                h1[:, t, :], start=(t == 0), stop=(t == H1 // P - 1))
                    last.then_inc(h2_done, 1)
                for t in range(H2 // P):
                    pe.wait_ge(h2_copied, h * (H2 // P) + t + 1)
                    last = nc.tensor.matmul(t_ps[0:1, 1, 0, :], w3_sb[:, t:t + 1], h2[:, t, :],
                                            start=(t == 0), stop=(t == H2 // P - 1))
                last.then_inc(y_done, 1)


def kernel(dense_ctx, ids, W_top1, b_top1, W_top2, b_top2, W_top3, L0_rec_kernel, **tables):
    import numpy as np
    import concourse.bacc as bacc
    from concourse.bass_utils import run_bass_kernel_spmd

    k_epf = np.ascontiguousarray(np.asarray(L0_rec_kernel).transpose(2, 1, 0))
    w1 = np.asarray(W_top1)
    pairs = FIELDS * (FIELDS - 1) // 2
    kchunks = np.zeros((EMBED, CHUNKS, 2, EMBED), k_epf.dtype)
    w1_rows = np.zeros((ZT, P, H1), w1.dtype)
    sel = np.zeros((P, 62), np.float32)
    sel[:EMBED, 30] = 1
    sel[EMBED:, 31] = 1
    sel_last = np.zeros((P, PACKS, 32), np.float32)
    for k in range(PACKS):
        for i in range(2 * k + 1):
            c = chunk_of(k, i)
            tile, group, pos = z_slot(c)
            row = 32 * group + 2 * pos
            for half, j in enumerate((2 * k, 2 * k + 1)):
                if i == j:
                    w1_rows[tile, row + half] = w1[pairs + k]
                    continue
                pair = i * (2 * FIELDS - 1 - i) // 2 + (j - i - 1)
                kchunks[:, c, half] = k_epf[:, pair]
                w1_rows[tile, row + half] = w1[pair]
            if i == 2 * k:
                sel_last[k, k, 2 * pos] = 1
                sel_last[EMBED:, k, 2 * pos + 1] = 1
    dense = np.zeros((EMBED, BATCH), np.asarray(dense_ctx).dtype)
    dense[:DENSE] = np.asarray(dense_ctx).T

    def tiles(a):
        a = np.asarray(a)
        return np.ascontiguousarray(a.reshape(-1, P, a.shape[1]).transpose(1, 0, 2))

    arrays = {
        "ids": np.ascontiguousarray(np.asarray(ids).reshape(BATCH // P, P, FIELDS).transpose(1, 0, 2)),
        "kchunks": np.ascontiguousarray(kchunks.reshape(EMBED, GROUPS, GC * P).transpose(1, 0, 2)),
        "dense": dense,
        "w1": np.ascontiguousarray(w1_rows.transpose(1, 0, 2)),
        "b1": np.ascontiguousarray(np.asarray(b_top1).reshape(-1, P).T),
        "w2": tiles(W_top2),
        "b2": np.ascontiguousarray(np.asarray(b_top2).reshape(-1, P).T),
        "w3": np.ascontiguousarray(np.asarray(W_top3).reshape(-1, P).T),
        "sel": sel,
        "sel_last": sel_last,
        "ident": np.eye(P, dtype=np.float32),
    }
    for f in range(FIELDS):
        arrays[f"tbl_{f}"] = np.ascontiguousarray(tables[f"tbl_{f}"])

    nc = bacc.Bacc("TRN2", target_bir_lowering=False, num_devices=1)
    aps = {n: nc.dram_tensor(n, a.shape, mybir.dt.from_np(a.dtype), kind="ExternalInput").ap()
           for n, a in arrays.items()}
    y = nc.dram_tensor("y", (1, BATCH), mybir.dt.float32, kind="ExternalOutput").ap()
    build(nc, tables=[aps.pop(f"tbl_{f}") for f in range(FIELDS)], y=y, **aps)
    r = run_bass_kernel_spmd(nc, [arrays], core_ids=[0])
    return r.results[0]["y"].reshape(BATCH, 1)
```

```python
import concourse.bass as bass
from concourse import mybir
from contextlib import ExitStack

BATCH, FIELDS, EMBED, DENSE = 1024, 32, 64, 16
H1, H2 = 512, 256
P = 128
HALVES = 2
HB = BATCH // HALVES
BT = HB // P
PACKS = FIELDS // 2
GC = 4
CHUNKS = PACKS * PACKS
GROUPS = CHUNKS // GC
TILE_CHUNKS = P // 2
ZT = CHUNKS // TILE_CHUNKS
KRING = 4
RAW = 8
SPLIT_LEAD = 5
X_LEAD = 3
Q_LEAD = 2
PRING = 4
POOL_FROM = 20


CREDIT = 1


def chunk_of(k, i):
    return k * k + i


def z_slot(c):
    return c // TILE_CHUNKS, c % 4, (c // 4) % 16


UNITS = [(k, tuple(i for i in (m, m + 1) if i <= 2 * k)) for k in range(PACKS) for m in range(0, 2 * k + 1, 2)]
NU = len(UNITS)
FIRST_UNIT = [min(u for u, (k, _) in enumerate(UNITS) if k == kk) for kk in range(PACKS)]
UNIT_OF_CHUNK = {chunk_of(k, i): u for u, (k, ii) in enumerate(UNITS) for i in ii}


def groups_due(u):
    def reach(v):
        return min(GROUPS, chunk_of(UNITS[v][0], UNITS[v][1][0]) // GC + 3)
    return range(reach(u - 1) if u else 0, reach(u))


def packs_due(u, lead):
    out = [0] if u == 0 else []
    k = UNITS[u][0]
    if k + 1 < PACKS and u == max(FIRST_UNIT[k], FIRST_UNIT[k + 1] - lead):
        out.append(k + 1)
    return out


def on_pool(g):
    return g >= POOL_FROM and g % 2 == 1


def lo_count(g):
    return sum(on_pool(x) == on_pool(g) for x in range(g + 1))


LO_PER_HALF = {p: sum(on_pool(g) == p for g in range(GROUPS)) for p in (False, True)}


def seen(h, per_half, v):
    if isinstance(h, int):
        return max(0, h * per_half + v)
    return h * per_half + v if v >= 0 else h * (per_half + v)


def build(nc, ids, tables, kchunks, dense, w1, b1, w2, b2, w3, sel, sel_last, ident, fold, y):
    fp32, f32r, i32 = mybir.dt.float32, mybir.dt.float32r, mybir.dt.int32
    ALU, ACT = mybir.AluOpType, mybir.ActivationFunctionType
    ctx = ExitStack()
    with ctx:
        def sb(name, shape, dt=fp32):
            return ctx.enter_context(nc.sbuf_tensor(name, shape, dt))

        def sem(name):
            return ctx.enter_context(nc.semaphore(name))

        ids_sb = sb("ids_sb", [P, BATCH // P, FIELDS], i32)
        ident_sb = sb("ident_sb", [P, P])
        fold_sb = sb("fold_sb", [P, 3 * EMBED])
        fold_r = sb("fold_r", [P, 3 * EMBED], f32r)
        ident_r = sb("ident_r", [P, P], f32r)
        sel_sb = sb("sel_sb", [P, 62])
        sel_last_sb = sb("sel_last_sb", [P, PACKS, 32])
        w1_sb = sb("w1_sb", [P, ZT, H1])
        w2_sb = sb("w2_sb", [P, H1 // P, H2])
        w3_sb = sb("w3_sb", [P, H2 // P])
        b1_sb = sb("b1_sb", [P, H1 // P])
        b2_sb = sb("b2_sb", [P, H2 // P])
        raw = sb("raw", [P, RAW, BT, 2, EMBED])
        parts = sb("parts", [P, BT, 2, 2, EMBED], f32r)
        xhl = sb("xhl", [P, FIELDS, HB], f32r)
        q = sb("q", [P, PACKS, HB])
        kraw = sb("kraw", [P, KRING, GC * P])
        khi = sb("khi", [P, KRING, GC * P], f32r)
        klo = sb("klo", [P, KRING, GC * P], f32r)
        prod = sb("prod", [P, PRING, 2, HB])
        prod_last = sb("prod_last", [P, 2, HB])
        zt = sb("zt", [P, ZT, HB])
        h1 = sb("h1", [P, H1 // P, HB])
        h2 = sb("h2", [P, H2 // P, HB])
        y_sb = sb("y_sb", [1, BATCH])

        t_ps = ctx.enter_context(nc.psum_tensor("t_ps", [P, 2, 2, HB], fp32))
        prep_ps = ctx.enter_context(nc.psum_tensor("prep_ps", [P, 2, HB], fp32))
        z_ps = ctx.enter_context(nc.psum_tensor("z_ps", [P, 2, HB], fp32))

        ids_in, consts_in, weights_in = sem("ids_in"), sem("consts_in"), sem("weights_in")
        dense_in = sem("dense_in")
        kraw_in = [sem(f"kraw_in{s}") for s in range(KRING)]
        gathered = [sem(f"gathered{s}") for s in range(RAW)]
        ident_done = sem("ident_done")
        xhi_done, xlo_done = sem("xhi_done"), sem("xlo_done")
        transposed, prep_copied = sem("transposed"), sem("prep_copied")
        khi_done, klo_dve, klo_pool = sem("khi_done"), sem("klo_dve"), sem("klo_pool")
        t_done, prod_done, summed, z_copied = sem("t_done"), sem("prod_done"), sem("summed"), sem("z_copied")
        h1_done, h1_copied, h2_done, h2_copied = sem("h1_done"), sem("h1_copied"), sem("h2_done"), sem("h2_copied")
        y_done, y_copied, y_stored = sem("y_done"), sem("y_copied"), sem("y_stored")

        block = ctx.enter_context(nc.Block())

        @block.sync
        def _(sp):
            sp.dma_start(ids_sb[:], ids).then_inc(ids_in, 16)

            def load_group(h, g, slot, first_g):
                last = (first_g - 1) * KRING + slot
                pooled = on_pool(last % GROUPS)
                if first_g:
                    per_round = sum(on_pool(last + n) == pooled for n in range(KRING))
                    count = h * LO_PER_HALF[pooled] + (g - first_g) * per_round + lo_count(last)
                else:
                    count = seen(h, LO_PER_HALF[pooled], lo_count(last % GROUPS) - LO_PER_HALF[pooled])
                sp.wait_ge(klo_pool if pooled else klo_dve, CREDIT + count)
                for lane in (0, EMBED):
                    sp.dma_start(kraw[lane:lane + EMBED, slot, :],
                                 kchunks[bass.ds(g * KRING + slot, 1), :, :].rearrange("g e n -> e (g n)")
                                 ).then_inc(kraw_in[slot], 16)

            with sp.Fori(0, HALVES) as h:
                for slot in range(KRING):
                    load_group(h, 0, slot, 0)
                sp.wait_ge(summed, CREDIT + h * NU)
                for slot in range(2):
                    sp.dma_start(prod_last[0:EMBED, slot, :], dense[:, bass.ds(h * HB, HB)]).then_inc(dense_in, 16)
                for begin, end in ((1, POOL_FROM // KRING + 1), (POOL_FROM // KRING + 1, GROUPS // KRING)):
                    with sp.Fori(begin, end) as g:
                        for slot in range(KRING):
                            load_group(h, g, slot, begin)

        @block.gpsimd
        def _(pool):
            def gather(pack):
                h, k = divmod(pack, PACKS)
                if pack >= RAW:
                    old = pack - RAW
                    pool.wait_ge(xlo_done, old + 1)
                for f in range(2):
                    for t in range(BT):
                        nc.gpsimd.indirect_dma_start(
                            raw[:, pack % RAW, t, f, :], None, tables[2 * k + f],
                            bass.IndirectOffsetOnAxis(ap=ids_sb[:, h * BT + t, 2 * k + f:2 * k + f + 1], axis=0),
                        ).then_inc(gathered[pack % RAW], 16)

            pool.sem_inc(klo_pool, CREDIT)
            pool.wait_ge(ids_in, 16)
            issued = 0
            for h in range(HALVES):
                for u in range(NU):
                    k = UNITS[u][0]
                    target = PACKS * h + (min(k + RAW, k + 3 + 2 * max(0, k - 6)) if h == 0 else k + RAW)
                    target = min(target, HALVES * PACKS)
                    if u == 0 and h == 0:
                        target = 2
                    for g in groups_due(u):
                        if on_pool(g):
                            n = h * GROUPS + g
                            pool.wait_ge(khi_done, n + 1)
                            nc.gpsimd.tensor_tensor(klo[:, g % KRING, :], kraw[:, g % KRING, :],
                                                    khi[:, g % KRING, :].bitcast(fp32),
                                                    ALU.subtract).then_inc(klo_pool, 1)
                    while issued < target:
                        gather(issued)
                        issued += 1

        @block.scalar
        def _(act):
            act.sem_inc(y_copied, CREDIT)
            act.dma_start(ident_sb[:], ident).then_inc(consts_in, 16)
            act.dma_start(fold_sb[:], fold).then_inc(consts_in, 16)
            act.dma_start(sel_sb[:], sel).then_inc(consts_in, 16)
            act.dma_start(sel_last_sb[:], sel_last).then_inc(consts_in, 16)
            for dst, src in ((w1_sb, w1), (w2_sb, w2), (w3_sb, w3), (b1_sb, b1), (b2_sb, b2)):
                act.dma_start(dst[:], src).then_inc(weights_in, 16)

            act.wait_ge(consts_in, 64)
            nc.scalar.activation(ident_r[:], ident_sb[:], ACT.Copy).then_inc(ident_done, 1)
            nc.scalar.activation(fold_r[:], fold_sb[:], ACT.Copy).then_inc(ident_done, 1)

            def split_group(h, g):
                act.wait_ge(kraw_in[g % KRING], h * (32 * GROUPS // KRING) + 32 * (g // KRING + 1))
                unit = UNIT_OF_CHUNK[(g - KRING) % GROUPS * GC + GC - 1]
                used = seen(h, NU, unit + 1 - (NU if g < KRING else 0))
                if not isinstance(used, int) or used:
                    act.wait_ge(t_done, used)
                nc.scalar.activation(khi[:, g % KRING, :], kraw[:, g % KRING, :], ACT.Copy).then_inc(khi_done, 1)

            def split_pack(h, k):
                act.wait_ge(gathered[k % RAW], h * (128 * PACKS // RAW) + 128 * (k // RAW + 1))
                act.wait_ge(transposed, CREDIT + seen(h, 3 * PACKS, 3 * k - 1))
                nc.scalar.activation(parts[:, :, :, 0, :], raw[:, k % RAW], ACT.Copy).then_inc(xhi_done, 1)

            def copy_prep(h, k, j):
                act.wait_ge(transposed, CREDIT + h * (3 * PACKS) + 3 * k + j + 1)
                dst = q[:, k, :] if j == 2 else xhl[:, 2 * k + j, :]
                nc.scalar.activation(dst, prep_ps[:, (3 * k + j) % 2, :], ACT.Copy).then_inc(prep_copied, 1)

            def copy_z(h, t):
                act.wait_ge(summed, CREDIT + h * NU + UNIT_OF_CHUNK[(t + 1) * TILE_CHUNKS - 1] + 1)
                nc.scalar.activation(zt[:, t, :], z_ps[:, t % 2, :], ACT.Copy).then_inc(z_copied, 1)

            z_at = {min(NU - 1, UNIT_OF_CHUNK[(t + 1) * TILE_CHUNKS - 1] + 4): t for t in range(ZT - 1)}
            def splits_and_copies(h, u):
                for g in groups_due(u):
                    split_group(h, g)
                splits, xs, qs = (packs_due(u, lead) for lead in (SPLIT_LEAD, X_LEAD, Q_LEAD))
                for k in sorted({*splits, *xs, *qs}):
                    if k in splits:
                        split_pack(h, k)
                    if k in xs:
                        copy_prep(h, k, 0)
                        copy_prep(h, k, 1)
                    if k in qs:
                        copy_prep(h, k, 2)

            splits_and_copies(0, 0)
            with act.Fori(0, HALVES) as h:
                for u in range(NU):
                    if u:
                        splits_and_copies(h, u)
                    if u in z_at:
                        copy_z(h, z_at[u])
                copy_z(h, ZT - 1)
                with act.If(h < HALVES - 1):
                    splits_and_copies(h + 1, 0)
                act.wait_ge(weights_in, 80)
                for m in range(H1 // P):
                    act.wait_ge(h1_done, h * (H1 // P) + m + 1)
                    nc.scalar.activation(h1[:, m, :], t_ps[:, m // 2, m % 2, :], ACT.Relu,
                                         bias=b1_sb[:, m:m + 1]).then_inc(h1_copied, 1)
                for m in range(H2 // P):
                    act.wait_ge(h2_done, h * (H2 // P) + m + 1)
                    nc.scalar.activation(h2[:, m, :], t_ps[:, 0, m, :], ACT.Relu,
                                         bias=b2_sb[:, m:m + 1]).then_inc(h2_copied, 1)
                act.wait_ge(y_done, h + 1)
                nc.scalar.activation(y_sb[:, bass.ds(h * HB, HB)], t_ps[0:1, 1, 0, :], ACT.Copy).then_inc(y_copied, 1)
                act.wait_ge(y_copied, CREDIT + h + 1)
                act.dma_start(y[:, bass.ds(h * HB, HB)], y_sb[:, bass.ds(h * HB, HB)]).then_inc(y_stored, 16)
            act.wait_ge(y_stored, 16 * HALVES)

        @block.vector
        def _(dve):
            def split_pack(h, k):
                dve.wait_ge(xhi_done, h * PACKS + k + 1)
                nc.vector.tensor_tensor(parts[:, :, :, 1, :], raw[:, k % RAW], parts[:, :, :, 0, :].bitcast(fp32),
                                        ALU.subtract).then_inc(xlo_done, 1)

            def split_group(h, g):
                dve.wait_ge(khi_done, h * GROUPS + g + 1)
                nc.vector.tensor_tensor(klo[:, g % KRING, :], kraw[:, g % KRING, :],
                                        khi[:, g % KRING, :].bitcast(fp32), ALU.subtract).then_inc(klo_dve, 1)

            def multiply(h, u):
                k, chunk_is = UNITS[u]
                dve.wait_ge(t_done, h * NU + u + 1)
                if len(chunk_is) == 2:
                    dve.wait_ge(summed, CREDIT + seen(h, NU, u - PRING + 1))
                    nc.vector.tensor_tensor(prod[:, u % PRING], t_ps[:, u % 2],
                                            q[:, k:k + 1, :].broadcast_to([P, 2, HB]), ALU.mult).then_inc(prod_done, 1)
                else:
                    if k >= 2:
                        dve.wait_ge(summed, CREDIT + h * NU + FIRST_UNIT[k - 1])
                    nc.vector.tensor_tensor(prod_last[EMBED:P, k % 2, :], t_ps[EMBED:P, u % 2, 0, :],
                                            q[EMBED:P, k, :], ALU.mult).then_inc(prod_done, 1)

            def splits(h, u):
                for g in groups_due(u):
                    if not on_pool(g):
                        split_group(h, g)
                for k in packs_due(u, SPLIT_LEAD):
                    split_pack(h, k)

            dve.sem_inc(klo_dve, CREDIT)
            dve.sem_inc(prod_done, CREDIT)
            splits(0, 0)
            with dve.Fori(0, HALVES) as h:
                for u in range(NU):
                    if u:
                        splits(h, u)
                    multiply(h, u)
                with dve.If(h < HALVES - 1):
                    splits(h + 1, 0)

        @block.tensor
        def _(pe):
            def transpose_x(h, k):
                for j in range(2):
                    if 3 * k + j >= 2:
                        pe.wait_ge(prep_copied, h * (3 * PACKS) + 3 * k + j - 1)
                    if j == 0:
                        pe.wait_ge(xlo_done, h * PACKS + k + 1)
                    for t in range(BT):
                        last = nc.tensor.matmul(prep_ps[:, (3 * k + j) % 2, t * P:(t + 1) * P],
                                                parts[:, t, j, :, :], ident_r[:], start=True, stop=True)
                    last.then_inc(transposed, 1)

            def fold_q(h, k):
                pe.wait_ge(prep_copied, h * (3 * PACKS) + 3 * k + 2)
                for j in range(2):
                    last = nc.tensor.matmul(prep_ps[:, (3 * k + 2) % 2, :], fold_r[:, (1 - j) * EMBED:(1 - j) * EMBED + P],
                                            xhl[:, 2 * k + j, :], start=(j == 0), stop=(j == 1))
                last.then_inc(transposed, 1)

            def prepare(h, u):
                xs, qs = packs_due(u, X_LEAD), packs_due(u, Q_LEAD)
                for k in sorted({*xs, *qs}):
                    if k in xs:
                        transpose_x(h, k)
                    if k in qs:
                        fold_q(h, k)

            def bilinear(h, u):
                k, chunk_is = UNITS[u]
                if u == FIRST_UNIT[k]:
                    pe.wait_ge(prep_copied, h * (3 * PACKS) + 3 * k + 3)
                pe.wait_ge(prod_done, CREDIT + seen(h, NU, u - 1))
                for n, i in enumerate(chunk_is):
                    c = chunk_of(k, i)
                    g, at = divmod(c, GC)
                    if at == 0:
                        pe.wait_ge(klo_pool if on_pool(g) else klo_dve,
                                   CREDIT + h * LO_PER_HALF[on_pool(g)] + lo_count(g))
                    for part, w in enumerate((khi, klo)):
                        last = nc.tensor.matmul(t_ps[:, u % 2, n, :], w[:, g % KRING, at * P:(at + 1) * P],
                                                xhl[:, i, :], start=(part == 0), stop=(part == 1))
                last.then_inc(t_done, 1)

            def feature_sums(h, u):
                k, chunk_is = UNITS[u]
                pe.wait_ge(prod_done, CREDIT + h * NU + u + 1)
                for n, i in enumerate(chunk_is):
                    tile, group, pos = z_slot(chunk_of(k, i))
                    if chunk_of(k, i) % TILE_CHUNKS == 0 and tile >= 2:
                        pe.wait_ge(z_copied, h * ZT + tile - 1)
                    last_chunk = i == 2 * k
                    w = sel_last_sb[:, k, :] if last_chunk else sel_sb[:, 30 - 2 * pos:62 - 2 * pos]
                    src = prod_last[:, k % 2, :] if last_chunk else prod[:, u % PRING, n, :]
                    last = nc.tensor.matmul(z_ps[32 * group:32 * group + 32, tile % 2, :], w, src,
                                            start=(pos == 0), stop=(pos == 15))
                last.then_inc(summed, 1)

            pe.sem_inc(summed, CREDIT)
            pe.sem_inc(transposed, CREDIT)
            pe.wait_ge(consts_in, 64)
            pe.wait_ge(ident_done, 2)
            prepare(0, 0)
            with pe.Fori(0, HALVES) as h:
                for u in range(NU):
                    if u:
                        prepare(h, u)
                    if u == 0:
                        pe.wait_ge(dense_in, h * 32 + 32)
                    if u == 1:
                        pe.wait_ge(y_copied, CREDIT + h)
                    bilinear(h, u)
                    if u % 2 and u >= 3:
                        feature_sums(h, u - 3)
                        feature_sums(h, u - 2)
                feature_sums(h, NU - 2)
                feature_sums(h, NU - 1)
                with pe.If(h < HALVES - 1):
                    prepare(h + 1, 0)

                pe.wait_ge(weights_in, 80)
                pe.wait_ge(z_copied, h * ZT + ZT)
                for m in range(H1 // P):
                    for t in range(ZT):
                        last = nc.tensor.matmul(t_ps[:, m // 2, m % 2, :], w1_sb[:, t, m * P:(m + 1) * P],
                                                zt[:, t, :], start=(t == 0), stop=(t == ZT - 1))
                    last.then_inc(h1_done, 1)
                for m in range(H2 // P):
                    for t in range(H1 // P):
                        if m == 0:
                            pe.wait_ge(h1_copied, h * (H1 // P) + t + 1)
                        last = nc.tensor.matmul(t_ps[:, 0, m, :], w2_sb[:, t, m * P:(m + 1) * P],
                                                h1[:, t, :], start=(t == 0), stop=(t == H1 // P - 1))
                    last.then_inc(h2_done, 1)
                for t in range(H2 // P):
                    pe.wait_ge(h2_copied, h * (H2 // P) + t + 1)
                    last = nc.tensor.matmul(t_ps[0:1, 1, 0, :], w3_sb[:, t:t + 1], h2[:, t, :],
                                            start=(t == 0), stop=(t == H2 // P - 1))
                last.then_inc(y_done, 1)


def kernel(dense_ctx, ids, W_top1, b_top1, W_top2, b_top2, W_top3, L0_rec_kernel, **tables):
    import numpy as np
    import concourse.bacc as bacc
    from concourse.bass_utils import run_bass_kernel_spmd

    k_epf = np.ascontiguousarray(np.asarray(L0_rec_kernel).transpose(2, 1, 0))
    w1 = np.asarray(W_top1)
    pairs = FIELDS * (FIELDS - 1) // 2
    kchunks = np.zeros((EMBED, CHUNKS, 2, EMBED), k_epf.dtype)
    w1_rows = np.zeros((ZT, P, H1), w1.dtype)
    sel = np.zeros((P, 62), np.float32)
    sel[:EMBED, 30] = 1
    sel[EMBED:, 31] = 1
    sel_last = np.zeros((P, PACKS, 32), np.float32)
    for k in range(PACKS):
        for i in range(2 * k + 1):
            c = chunk_of(k, i)
            tile, group, pos = z_slot(c)
            row = 32 * group + 2 * pos
            for half, j in enumerate((2 * k, 2 * k + 1)):
                if i == j:
                    w1_rows[tile, row + half] = w1[pairs + k]
                    continue
                pair = i * (2 * FIELDS - 1 - i) // 2 + (j - i - 1)
                kchunks[:, c, half] = k_epf[:, pair]
                w1_rows[tile, row + half] = w1[pair]
            if i == 2 * k:
                sel_last[k, k, 2 * pos] = 1
                sel_last[EMBED:, k, 2 * pos + 1] = 1
    fold = np.zeros((P, 3 * EMBED), np.float32)
    fold[:, EMBED:2 * EMBED] = np.tile(np.eye(EMBED, dtype=np.float32), (2, 1))
    dense = np.zeros((EMBED, BATCH), np.asarray(dense_ctx).dtype)
    dense[:DENSE] = np.asarray(dense_ctx).T

    def tiles(a):
        a = np.asarray(a)
        return np.ascontiguousarray(a.reshape(-1, P, a.shape[1]).transpose(1, 0, 2))

    arrays = {
        "ids": np.ascontiguousarray(np.asarray(ids).reshape(BATCH // P, P, FIELDS).transpose(1, 0, 2)),
        "kchunks": np.ascontiguousarray(kchunks.reshape(EMBED, GROUPS, GC * P).transpose(1, 0, 2)),
        "dense": dense,
        "w1": np.ascontiguousarray(w1_rows.transpose(1, 0, 2)),
        "b1": np.ascontiguousarray(np.asarray(b_top1).reshape(-1, P).T),
        "w2": tiles(W_top2),
        "b2": np.ascontiguousarray(np.asarray(b_top2).reshape(-1, P).T),
        "w3": np.ascontiguousarray(np.asarray(W_top3).reshape(-1, P).T),
        "sel": sel,
        "sel_last": sel_last,
        "fold": fold,
        "ident": np.eye(P, dtype=np.float32),
    }
    for f in range(FIELDS):
        arrays[f"tbl_{f}"] = np.ascontiguousarray(tables[f"tbl_{f}"])

    nc = bacc.Bacc("TRN2", target_bir_lowering=False, num_devices=1)
    aps = {n: nc.dram_tensor(n, a.shape, mybir.dt.from_np(a.dtype), kind="ExternalInput").ap()
           for n, a in arrays.items()}
    y = nc.dram_tensor("y", (1, BATCH), mybir.dt.float32, kind="ExternalOutput").ap()
    build(nc, tables=[aps.pop(f"tbl_{f}") for f in range(FIELDS)], y=y, **aps)
    r = run_bass_kernel_spmd(nc, [arrays], core_ids=[0])
    return r.results[0]["y"].reshape(BATCH, 1)
```

```python
import concourse.bass as bass
from concourse import mybir
from contextlib import ExitStack

BATCH, FIELDS, EMBED, DENSE = 1024, 32, 64, 16
H1, H2 = 512, 256
P = 128
HALVES = 2
HB = BATCH // HALVES
BT = HB // P
PACKS = FIELDS // 2
GC = 4
CHUNKS = PACKS * PACKS
GROUPS = CHUNKS // GC
TILE_CHUNKS = P // 2
ZT = CHUNKS // TILE_CHUNKS
KRING = 4
RAW = 8
SPLIT_LEAD = 5
X_LEAD = 3
Q_LEAD = 2
PRING = 4
POOL_FROM = 36
POOL_SLOTS = (0, 1, 2, 3)


CREDIT = 1


def chunk_of(k, i):
    return k * k + i


def z_slot(c):
    return c // TILE_CHUNKS, c % 4, (c // 4) % 16


UNITS = [(k, tuple(i for i in (m, m + 1) if i <= 2 * k)) for k in range(PACKS) for m in range(0, 2 * k + 1, 2)]
NU = len(UNITS)
FIRST_UNIT = [min(u for u, (k, _) in enumerate(UNITS) if k == kk) for kk in range(PACKS)]
UNIT_OF_CHUNK = {chunk_of(k, i): u for u, (k, ii) in enumerate(UNITS) for i in ii}


def groups_due(u):
    def reach(v):
        return min(GROUPS, chunk_of(UNITS[v][0], UNITS[v][1][0]) // GC + 3)
    return range(reach(u - 1) if u else 0, reach(u))


def preparations(u):
    if u == 0:
        return [[("split", 0), ("split", 1), ("x", 0)], [("split", 2), ("q", 0), ("x", 1)], [("q", 1), ("x", 2)]]
    due = [(k, what) for what, lead in (("split", SPLIT_LEAD), ("x", X_LEAD), ("q", Q_LEAD))
           for k in range(PACKS) if u == max(0, FIRST_UNIT[k] - lead)]
    return [[(what, k) for k, what in sorted(due, key=lambda d: d[0])]]


def on_pool(g):
    return g >= POOL_FROM and g % KRING in POOL_SLOTS


def lo_count(g):
    return sum(on_pool(x) == on_pool(g) for x in range(g + 1))


LO_PER_HALF = {p: sum(on_pool(g) == p for g in range(GROUPS)) for p in (False, True)}


def seen(h, per_half, v):
    if isinstance(h, int):
        return max(0, h * per_half + v)
    return h * per_half + v if v >= 0 else h * (per_half + v)


def build(nc, ids, tables, kchunks, dense, w1, b1, w2, b2, w3, sel, sel_last, ident, fold, y):
    fp32, f32r, i32 = mybir.dt.float32, mybir.dt.float32r, mybir.dt.int32
    ALU, ACT = mybir.AluOpType, mybir.ActivationFunctionType
    ctx = ExitStack()
    with ctx:
        def sb(name, shape, dt=fp32):
            return ctx.enter_context(nc.sbuf_tensor(name, shape, dt))

        def sem(name):
            return ctx.enter_context(nc.semaphore(name))

        ids_sb = sb("ids_sb", [P, BATCH // P, FIELDS], i32)
        ident_sb = sb("ident_sb", [P, P])
        fold_sb = sb("fold_sb", [P, 3 * EMBED])
        fold_r = sb("fold_r", [P, 3 * EMBED], f32r)
        ident_r = sb("ident_r", [P, P], f32r)
        sel_sb = sb("sel_sb", [P, 62])
        sel_last_sb = sb("sel_last_sb", [P, PACKS, 32])
        w1_sb = sb("w1_sb", [P, ZT, H1])
        w2_sb = sb("w2_sb", [P, H1 // P, H2])
        w3_sb = sb("w3_sb", [P, H2 // P])
        b1_sb = sb("b1_sb", [P, H1 // P])
        b2_sb = sb("b2_sb", [P, H2 // P])
        raw = sb("raw", [P, RAW, BT, 2, EMBED])
        parts = sb("parts", [P, 2, BT, 2, 2, EMBED], f32r)
        xhl = sb("xhl", [P, FIELDS, HB], f32r)
        q = sb("q", [P, PACKS, HB])
        kraw = sb("kraw", [P, KRING, GC * P])
        khi = sb("khi", [P, KRING, GC * P], f32r)
        klo = sb("klo", [P, KRING, GC * P], f32r)
        prod = sb("prod", [P, PRING, 2, HB])
        prod_last = sb("prod_last", [P, 2, HB])
        zt = sb("zt", [P, ZT, HB])
        h1 = sb("h1", [P, H1 // P, HB])
        h2 = sb("h2", [P, H2 // P, HB])
        y_sb = sb("y_sb", [1, BATCH])

        t_ps = ctx.enter_context(nc.psum_tensor("t_ps", [P, 2, 2, HB], fp32))
        prep_ps = ctx.enter_context(nc.psum_tensor("prep_ps", [P, 2, HB], fp32))
        z_ps = ctx.enter_context(nc.psum_tensor("z_ps", [P, 2, HB], fp32))

        ids_in, consts_in, weights_in = sem("ids_in"), sem("consts_in"), sem("weights_in")
        dense_in = sem("dense_in")
        kraw_in = [sem(f"kraw_in{s}") for s in range(KRING)]
        gathered = [sem(f"gathered{s}") for s in range(RAW)]
        ident_done = sem("ident_done")
        xhi_done, xlo_done = sem("xhi_done"), sem("xlo_done")
        transposed, prep_copied = sem("transposed"), sem("prep_copied")
        khi_done, klo_dve, klo_pool = sem("khi_done"), sem("klo_dve"), sem("klo_pool")
        t_done, prod_done, summed, z_copied = sem("t_done"), sem("prod_done"), sem("summed"), sem("z_copied")
        h1_done, h1_copied, h2_done, h2_copied = sem("h1_done"), sem("h1_copied"), sem("h2_done"), sem("h2_copied")
        y_done, y_copied, y_stored = sem("y_done"), sem("y_copied"), sem("y_stored")

        block = ctx.enter_context(nc.Block())

        @block.sync
        def _(sp):
            sp.dma_start(ids_sb[:], ids).then_inc(ids_in, 16)

            def load_group(h, g, slot, first_g):
                last = (first_g - 1) * KRING + slot
                pooled = on_pool(last % GROUPS)
                if first_g:
                    per_round = sum(on_pool(last + n) == pooled for n in range(KRING))
                    count = h * LO_PER_HALF[pooled] + (g - first_g) * per_round + lo_count(last)
                else:
                    count = seen(h, LO_PER_HALF[pooled], lo_count(last % GROUPS) - LO_PER_HALF[pooled])
                sp.wait_ge(klo_pool if pooled else klo_dve, CREDIT + count)
                for lane in (0, EMBED):
                    sp.dma_start(kraw[lane:lane + EMBED, slot, :],
                                 kchunks[bass.ds(g * KRING + slot, 1), :, :].rearrange("g e n -> e (g n)")
                                 ).then_inc(kraw_in[slot], 16)

            with sp.Fori(0, HALVES) as h:
                for slot in range(KRING):
                    load_group(h, 0, slot, 0)
                sp.wait_ge(summed, CREDIT + h * NU)
                for slot in range(2):
                    sp.dma_start(prod_last[0:EMBED, slot, :], dense[:, bass.ds(h * HB, HB)]).then_inc(dense_in, 16)
                for begin, end in ((1, POOL_FROM // KRING + 1), (POOL_FROM // KRING + 1, GROUPS // KRING)):
                    with sp.Fori(begin, end) as g:
                        for slot in range(KRING):
                            load_group(h, g, slot, begin)

        @block.gpsimd
        def _(pool):
            def gather(pack, n):
                h, k = divmod(pack, PACKS)
                f, t = divmod(n, BT)
                if pack >= RAW and n == 0:
                    pool.wait_ge(xlo_done, pack - RAW + 1)
                nc.gpsimd.indirect_dma_start(
                    raw[:, pack % RAW, t, f, :], None, tables[2 * k + f],
                    bass.IndirectOffsetOnAxis(ap=ids_sb[:, h * BT + t, 2 * k + f:2 * k + f + 1], axis=0),
                ).then_inc(gathered[pack % RAW], 16)

            def ahead(h, k):
                return RAW if h else min(RAW, 4 + max(0, k - 6))

            pool.sem_inc(klo_pool, CREDIT)
            pool.wait_ge(ids_in, 16)
            issued = 0
            for h in range(HALVES):
                for u in range(NU):
                    k, done = UNITS[u][0], u - FIRST_UNIT[UNITS[u][0]] + 1
                    for g in groups_due(u):
                        if on_pool(g):
                            pool.wait_ge(khi_done, h * GROUPS + g + 1)
                            nc.gpsimd.tensor_tensor(klo[:, g % KRING, :], kraw[:, g % KRING, :],
                                                    khi[:, g % KRING, :].bitcast(fp32),
                                                    ALU.subtract).then_inc(klo_pool, 1)
                    before, after = (PACKS * h + x + ahead(h, x) for x in (k - 1, k))
                    share = before + (after - before) * done / (k + 1)
                    while issued < min(int(share * 2 * BT), HALVES * PACKS * 2 * BT):
                        gather(*divmod(issued, 2 * BT))
                        issued += 1

        @block.scalar
        def _(act):
            act.sem_inc(y_copied, CREDIT)
            act.dma_start(ident_sb[:], ident).then_inc(consts_in, 16)
            act.dma_start(fold_sb[:], fold).then_inc(consts_in, 16)
            act.dma_start(sel_sb[:], sel).then_inc(consts_in, 16)
            act.dma_start(sel_last_sb[:], sel_last).then_inc(consts_in, 16)
            for dst, src in ((w1_sb, w1), (w2_sb, w2), (w3_sb, w3), (b1_sb, b1), (b2_sb, b2)):
                act.dma_start(dst[:], src).then_inc(weights_in, 16)

            act.wait_ge(consts_in, 64)
            nc.scalar.activation(ident_r[:], ident_sb[:], ACT.Copy).then_inc(ident_done, 1)
            nc.scalar.activation(fold_r[:], fold_sb[:], ACT.Copy).then_inc(ident_done, 1)

            def split_group(h, g):
                act.wait_ge(kraw_in[g % KRING], h * (32 * GROUPS // KRING) + 32 * (g // KRING + 1))
                unit = UNIT_OF_CHUNK[(g - KRING) % GROUPS * GC + GC - 1]
                used = seen(h, NU, unit + 1 - (NU if g < KRING else 0))
                if not isinstance(used, int) or used:
                    act.wait_ge(t_done, used)
                nc.scalar.activation(khi[:, g % KRING, :], kraw[:, g % KRING, :], ACT.Copy).then_inc(khi_done, 1)

            def split_pack(h, k):
                act.wait_ge(gathered[k % RAW], h * (128 * PACKS // RAW) + 128 * (k // RAW + 1))
                act.wait_ge(transposed, CREDIT + seen(h, 3 * PACKS, 3 * k - 4))
                nc.scalar.activation(parts[:, k % 2, :, :, 0, :], raw[:, k % RAW], ACT.Copy).then_inc(xhi_done, 1)

            def copy_prep(h, k, j):
                act.wait_ge(transposed, CREDIT + h * (3 * PACKS) + 3 * k + j + 1)
                dst = q[:, k, :] if j == 2 else xhl[:, 2 * k + j, :]
                nc.scalar.activation(dst, prep_ps[:, (3 * k + j) % 2, :], ACT.Copy).then_inc(prep_copied, 1)

            def copy_z(h, t):
                act.wait_ge(summed, CREDIT + h * NU + UNIT_OF_CHUNK[(t + 1) * TILE_CHUNKS - 1] + 1)
                nc.scalar.activation(zt[:, t, :], z_ps[:, t % 2, :], ACT.Copy).then_inc(z_copied, 1)

            z_at = {min(NU - 1, UNIT_OF_CHUNK[(t + 1) * TILE_CHUNKS - 1] + 4): t for t in range(ZT - 1)}
            def splits_and_copies(h, u):
                for g in groups_due(u):
                    split_group(h, g)
                for what, k in sum(preparations(u), []):
                    if what == "split":
                        split_pack(h, k)
                    elif what == "x":
                        copy_prep(h, k, 0)
                        copy_prep(h, k, 1)
                    else:
                        copy_prep(h, k, 2)

            splits_and_copies(0, 0)
            with act.Fori(0, HALVES) as h:
                for u in range(NU):
                    if u:
                        splits_and_copies(h, u)
                    if u in z_at:
                        copy_z(h, z_at[u])
                copy_z(h, ZT - 1)
                with act.If(h < HALVES - 1):
                    splits_and_copies(h + 1, 0)
                act.wait_ge(weights_in, 80)
                for m in range(H1 // P):
                    act.wait_ge(h1_done, h * (H1 // P) + m + 1)
                    nc.scalar.activation(h1[:, m, :], t_ps[:, m // 2, m % 2, :], ACT.Relu,
                                         bias=b1_sb[:, m:m + 1]).then_inc(h1_copied, 1)
                for m in range(H2 // P):
                    act.wait_ge(h2_done, h * (H2 // P) + m + 1)
                    nc.scalar.activation(h2[:, m, :], t_ps[:, 0, m, :], ACT.Relu,
                                         bias=b2_sb[:, m:m + 1]).then_inc(h2_copied, 1)
                act.wait_ge(y_done, h + 1)
                nc.scalar.activation(y_sb[:, bass.ds(h * HB, HB)], t_ps[0:1, 1, 0, :], ACT.Copy).then_inc(y_copied, 1)
                act.wait_ge(y_copied, CREDIT + h + 1)
                act.dma_start(y[:, bass.ds(h * HB, HB)], y_sb[:, bass.ds(h * HB, HB)]).then_inc(y_stored, 16)
            act.wait_ge(y_stored, 16 * HALVES)

        @block.vector
        def _(dve):
            def split_pack(h, k):
                dve.wait_ge(xhi_done, h * PACKS + k + 1)
                nc.vector.tensor_tensor(parts[:, k % 2, :, :, 1, :], raw[:, k % RAW],
                                        parts[:, k % 2, :, :, 0, :].bitcast(fp32), ALU.subtract).then_inc(xlo_done, 1)

            def split_group(h, g):
                dve.wait_ge(khi_done, h * GROUPS + g + 1)
                nc.vector.tensor_tensor(klo[:, g % KRING, :], kraw[:, g % KRING, :],
                                        khi[:, g % KRING, :].bitcast(fp32), ALU.subtract).then_inc(klo_dve, 1)

            def multiply(h, u):
                k, chunk_is = UNITS[u]
                dve.wait_ge(t_done, h * NU + u + 1)
                if len(chunk_is) == 2:
                    dve.wait_ge(summed, CREDIT + seen(h, NU, u - PRING + 1))
                    nc.vector.tensor_tensor(prod[:, u % PRING], t_ps[:, u % 2],
                                            q[:, k:k + 1, :].broadcast_to([P, 2, HB]), ALU.mult).then_inc(prod_done, 1)
                else:
                    if k >= 2:
                        dve.wait_ge(summed, CREDIT + h * NU + FIRST_UNIT[k - 1])
                    nc.vector.tensor_tensor(prod_last[EMBED:P, k % 2, :], t_ps[EMBED:P, u % 2, 0, :],
                                            q[EMBED:P, k, :], ALU.mult).then_inc(prod_done, 1)

            def splits(h, u):
                for g in groups_due(u):
                    if not on_pool(g):
                        split_group(h, g)
                for what, k in sum(preparations(u), []):
                    if what == "split":
                        split_pack(h, k)

            dve.sem_inc(klo_dve, CREDIT)
            dve.sem_inc(prod_done, CREDIT)
            splits(0, 0)
            with dve.Fori(0, HALVES) as h:
                for u in range(NU):
                    if u:
                        splits(h, u)
                    multiply(h, u)
                with dve.If(h < HALVES - 1):
                    splits(h + 1, 0)

        @block.tensor
        def _(pe):
            def transpose_x(h, k):
                for j in range(2):
                    if 3 * k + j >= 2:
                        pe.wait_ge(prep_copied, h * (3 * PACKS) + 3 * k + j - 1)
                    if j == 0:
                        pe.wait_ge(xlo_done, h * PACKS + k + 1)
                    for t in range(BT):
                        last = nc.tensor.matmul(prep_ps[:, (3 * k + j) % 2, t * P:(t + 1) * P],
                                                parts[:, k % 2, t, j, :, :], ident_r[:], start=True, stop=True)
                    last.then_inc(transposed, 1)

            def fold_q(h, k):
                pe.wait_ge(prep_copied, h * (3 * PACKS) + 3 * k + 2)
                for j in range(2):
                    last = nc.tensor.matmul(prep_ps[:, (3 * k + 2) % 2, :], fold_r[:, (1 - j) * EMBED:(1 - j) * EMBED + P],
                                            xhl[:, 2 * k + j, :], start=(j == 0), stop=(j == 1))
                last.then_inc(transposed, 1)

            def prepare(h, lot):
                for what, k in lot:
                    if what == "x":
                        transpose_x(h, k)
                    elif what == "q":
                        fold_q(h, k)

            def bilinear(h, u):
                k, chunk_is = UNITS[u]
                if u == FIRST_UNIT[k]:
                    pe.wait_ge(prep_copied, h * (3 * PACKS) + 3 * k + 3)
                pe.wait_ge(prod_done, CREDIT + seen(h, NU, u - 1))
                for n, i in enumerate(chunk_is):
                    c = chunk_of(k, i)
                    g, at = divmod(c, GC)
                    if at == 0:
                        pe.wait_ge(klo_pool if on_pool(g) else klo_dve,
                                   CREDIT + h * LO_PER_HALF[on_pool(g)] + lo_count(g))
                    for part, w in enumerate((khi, klo)):
                        last = nc.tensor.matmul(t_ps[:, u % 2, n, :], w[:, g % KRING, at * P:(at + 1) * P],
                                                xhl[:, i, :], start=(part == 0), stop=(part == 1))
                last.then_inc(t_done, 1)

            def feature_sums(h, u):
                k, chunk_is = UNITS[u]
                pe.wait_ge(prod_done, CREDIT + h * NU + u + 1)
                for n, i in enumerate(chunk_is):
                    tile, group, pos = z_slot(chunk_of(k, i))
                    if chunk_of(k, i) % TILE_CHUNKS == 0 and tile >= 2:
                        pe.wait_ge(z_copied, h * ZT + tile - 1)
                    last_chunk = i == 2 * k
                    w = sel_last_sb[:, k, :] if last_chunk else sel_sb[:, 30 - 2 * pos:62 - 2 * pos]
                    src = prod_last[:, k % 2, :] if last_chunk else prod[:, u % PRING, n, :]
                    last = nc.tensor.matmul(z_ps[32 * group:32 * group + 32, tile % 2, :], w, src,
                                            start=(pos == 0), stop=(pos == 15))
                last.then_inc(summed, 1)

            pe.sem_inc(summed, CREDIT)
            pe.sem_inc(transposed, CREDIT)
            pe.wait_ge(consts_in, 64)
            pe.wait_ge(ident_done, 2)
            for lot in preparations(0):
                prepare(0, lot)
            with pe.Fori(0, HALVES) as h:
                for u in range(NU):
                    if u:
                        prepare(h, sum(preparations(u), []))
                    if u == 0:
                        pe.wait_ge(dense_in, h * 32 + 32)
                    if u == 1:
                        pe.wait_ge(y_copied, CREDIT + h)
                    bilinear(h, u)
                    if u % 2 and u >= 3:
                        feature_sums(h, u - 3)
                        feature_sums(h, u - 2)
                feature_sums(h, NU - 2)
                feature_sums(h, NU - 1)

                pe.wait_ge(weights_in, 80)
                for t in range(ZT):
                    if t < len(preparations(0)):
                        with pe.If(h < HALVES - 1):
                            prepare(h + 1, preparations(0)[t])
                    pe.wait_ge(z_copied, h * ZT + t + 1)
                    for m in range(H1 // P):
                        last = nc.tensor.matmul(t_ps[:, m // 2, m % 2, :], w1_sb[:, t, m * P:(m + 1) * P],
                                                zt[:, t, :], start=(t == 0), stop=(t == ZT - 1))
                        if t == ZT - 1:
                            last.then_inc(h1_done, 1)
                for t in range(H1 // P):
                    pe.wait_ge(h1_copied, h * (H1 // P) + max(t + 1, H2 // P))
                    for m in range(H2 // P):
                        last = nc.tensor.matmul(t_ps[:, 0, m, :], w2_sb[:, t, m * P:(m + 1) * P],
                                                h1[:, t, :], start=(t == 0), stop=(t == H1 // P - 1))
                        if t == H1 // P - 1:
                            last.then_inc(h2_done, 1)
                for t in range(H2 // P):
                    pe.wait_ge(h2_copied, h * (H2 // P) + t + 1)
                    last = nc.tensor.matmul(t_ps[0:1, 1, 0, :], w3_sb[:, t:t + 1], h2[:, t, :],
                                            start=(t == 0), stop=(t == H2 // P - 1))
                last.then_inc(y_done, 1)


def kernel(dense_ctx, ids, W_top1, b_top1, W_top2, b_top2, W_top3, L0_rec_kernel, **tables):
    import numpy as np
    import concourse.bacc as bacc
    from concourse.bass_utils import run_bass_kernel_spmd

    k_epf = np.ascontiguousarray(np.asarray(L0_rec_kernel).transpose(2, 1, 0))
    w1 = np.asarray(W_top1)
    pairs = FIELDS * (FIELDS - 1) // 2
    kchunks = np.zeros((EMBED, CHUNKS, 2, EMBED), k_epf.dtype)
    w1_rows = np.zeros((ZT, P, H1), w1.dtype)
    sel = np.zeros((P, 62), np.float32)
    sel[:EMBED, 30] = 1
    sel[EMBED:, 31] = 1
    sel_last = np.zeros((P, PACKS, 32), np.float32)
    for k in range(PACKS):
        for i in range(2 * k + 1):
            c = chunk_of(k, i)
            tile, group, pos = z_slot(c)
            row = 32 * group + 2 * pos
            for half, j in enumerate((2 * k, 2 * k + 1)):
                if i == j:
                    w1_rows[tile, row + half] = w1[pairs + k]
                    continue
                pair = i * (2 * FIELDS - 1 - i) // 2 + (j - i - 1)
                kchunks[:, c, half] = k_epf[:, pair]
                w1_rows[tile, row + half] = w1[pair]
            if i == 2 * k:
                sel_last[k, k, 2 * pos] = 1
                sel_last[EMBED:, k, 2 * pos + 1] = 1
    fold = np.zeros((P, 3 * EMBED), np.float32)
    fold[:, EMBED:2 * EMBED] = np.tile(np.eye(EMBED, dtype=np.float32), (2, 1))
    dense = np.zeros((EMBED, BATCH), np.asarray(dense_ctx).dtype)
    dense[:DENSE] = np.asarray(dense_ctx).T

    def tiles(a):
        a = np.asarray(a)
        return np.ascontiguousarray(a.reshape(-1, P, a.shape[1]).transpose(1, 0, 2))

    arrays = {
        "ids": np.ascontiguousarray(np.asarray(ids).reshape(BATCH // P, P, FIELDS).transpose(1, 0, 2)),
        "kchunks": np.ascontiguousarray(kchunks.reshape(EMBED, GROUPS, GC * P).transpose(1, 0, 2)),
        "dense": dense,
        "w1": np.ascontiguousarray(w1_rows.transpose(1, 0, 2)),
        "b1": np.ascontiguousarray(np.asarray(b_top1).reshape(-1, P).T),
        "w2": tiles(W_top2),
        "b2": np.ascontiguousarray(np.asarray(b_top2).reshape(-1, P).T),
        "w3": np.ascontiguousarray(np.asarray(W_top3).reshape(-1, P).T),
        "sel": sel,
        "sel_last": sel_last,
        "fold": fold,
        "ident": np.eye(P, dtype=np.float32),
    }
    for f in range(FIELDS):
        arrays[f"tbl_{f}"] = np.ascontiguousarray(tables[f"tbl_{f}"])

    nc = bacc.Bacc("TRN2", target_bir_lowering=False, num_devices=1)
    aps = {n: nc.dram_tensor(n, a.shape, mybir.dt.from_np(a.dtype), kind="ExternalInput").ap()
           for n, a in arrays.items()}
    y = nc.dram_tensor("y", (1, BATCH), mybir.dt.float32, kind="ExternalOutput").ap()
    build(nc, tables=[aps.pop(f"tbl_{f}") for f in range(FIELDS)], y=y, **aps)
    r = run_bass_kernel_spmd(nc, [arrays], core_ids=[0])
    return r.results[0]["y"].reshape(BATCH, 1)
```
